# Optimizing a Trainium2 kernel written in Bass

```python
import numpy as np
import jax
import jax.numpy as jnp

def _softmax(x, axis=-1):
    return jax.nn.softmax(x, axis=axis)

def _gelu(x):
    return jax.nn.gelu(x, approximate=True)

def _silu(x):
    return jax.nn.silu(x)

def _sigmoid(x):
    return jax.nn.sigmoid(x)

def _layernorm(x, axis=-1, eps=1e-05):
    m = jnp.mean(x, axis=axis, keepdims=True)
    v = jnp.var(x, axis=axis, keepdims=True)
    return (x - m) / jnp.sqrt(v + eps)

def _scatter_add(tgt, idx, src, axis=0):
    return tgt.at[idx].add(src)

def _segment_sum(src, seg, n):
    return jax.ops.segment_sum(src, seg, n)
kernel_name = 'mk_dlrm_tower_d1_rec_r8_c3630b'

def setup_inputs(seed: int=0):
    np.random.seed(seed)
    _w = jnp.asarray

    def _rec_inputs():
        import jax
        import jax.numpy as jnp
        _tk = jax.random.key(seed)
        dense_ctx = jax.random.normal(jax.random.fold_in(_tk, 190), (2048, 16), jnp.float32)
        ids = jnp.stack([jax.random.randint(jax.random.fold_in(_tk, 200 + f), (2048,), 0, v, jnp.int32) for f, v in enumerate([12500, 1250, 1250, 125000, 1000, 125000, 12500, 1250, 1250, 12500, 12500, 12500, 1000, 1000, 1000, 1250, 125000, 1250, 1000, 1250, 1250, 1250, 12500, 125000, 12500, 1000, 1000, 125000, 12500, 12500, 1250, 1250, 125000, 1000, 125000, 1000, 12500, 125000, 1000])], axis=1)
        tbl_0 = 0.05 * jax.random.normal(jax.random.fold_in(_tk, 500 + 0), (12500, 16), jnp.float32)
        tbl_1 = 0.05 * jax.random.normal(jax.random.fold_in(_tk, 500 + 1), (1250, 16), jnp.float32)
        tbl_2 = 0.05 * jax.random.normal(jax.random.fold_in(_tk, 500 + 2), (1250, 16), jnp.float32)
        tbl_3 = 0.05 * jax.random.normal(jax.random.fold_in(_tk, 500 + 3), (125000, 16), jnp.float32)
        tbl_4 = 0.05 * jax.random.normal(jax.random.fold_in(_tk, 500 + 4), (1000, 16), jnp.float32)
        tbl_5 = 0.05 * jax.random.normal(jax.random.fold_in(_tk, 500 + 5), (125000, 16), jnp.float32)
        tbl_6 = 0.05 * jax.random.normal(jax.random.fold_in(_tk, 500 + 6), (12500, 16), jnp.float32)
        tbl_7 = 0.05 * jax.random.normal(jax.random.fold_in(_tk, 500 + 7), (1250, 16), jnp.float32)
        tbl_8 = 0.05 * jax.random.normal(jax.random.fold_in(_tk, 500 + 8), (1250, 16), jnp.float32)
        tbl_9 = 0.05 * jax.random.normal(jax.random.fold_in(_tk, 500 + 9), (12500, 16), jnp.float32)
        tbl_10 = 0.05 * jax.random.normal(jax.random.fold_in(_tk, 500 + 10), (12500, 16), jnp.float32)
        tbl_11 = 0.05 * jax.random.normal(jax.random.fold_in(_tk, 500 + 11), (12500, 16), jnp.float32)
        tbl_12 = 0.05 * jax.random.normal(jax.random.fold_in(_tk, 500 + 12), (1000, 16), jnp.float32)
        tbl_13 = 0.05 * jax.random.normal(jax.random.fold_in(_tk, 500 + 13), (1000, 16), jnp.float32)
        tbl_14 = 0.05 * jax.random.normal(jax.random.fold_in(_tk, 500 + 14), (1000, 16), jnp.float32)
        tbl_15 = 0.05 * jax.random.normal(jax.random.fold_in(_tk, 500 + 15), (1250, 16), jnp.float32)
        tbl_16 = 0.05 * jax.random.normal(jax.random.fold_in(_tk, 500 + 16), (125000, 16), jnp.float32)
        tbl_17 = 0.05 * jax.random.normal(jax.random.fold_in(_tk, 500 + 17), (1250, 16), jnp.float32)
        tbl_18 = 0.05 * jax.random.normal(jax.random.fold_in(_tk, 500 + 18), (1000, 16), jnp.float32)
        tbl_19 = 0.05 * jax.random.normal(jax.random.fold_in(_tk, 500 + 19), (1250, 16), jnp.float32)
        tbl_20 = 0.05 * jax.random.normal(jax.random.fold_in(_tk, 500 + 20), (1250, 16), jnp.float32)
        tbl_21 = 0.05 * jax.random.normal(jax.random.fold_in(_tk, 500 + 21), (1250, 16), jnp.float32)
        tbl_22 = 0.05 * jax.random.normal(jax.random.fold_in(_tk, 500 + 22), (12500, 16), jnp.float32)
        tbl_23 = 0.05 * jax.random.normal(jax.random.fold_in(_tk, 500 + 23), (125000, 16), jnp.float32)
        tbl_24 = 0.05 * jax.random.normal(jax.random.fold_in(_tk, 500 + 24), (12500, 16), jnp.float32)
        tbl_25 = 0.05 * jax.random.normal(jax.random.fold_in(_tk, 500 + 25), (1000, 16), jnp.float32)
        tbl_26 = 0.05 * jax.random.normal(jax.random.fold_in(_tk, 500 + 26), (1000, 16), jnp.float32)
        tbl_27 = 0.05 * jax.random.normal(jax.random.fold_in(_tk, 500 + 27), (125000, 16), jnp.float32)
        tbl_28 = 0.05 * jax.random.normal(jax.random.fold_in(_tk, 500 + 28), (12500, 16), jnp.float32)
        tbl_29 = 0.05 * jax.random.normal(jax.random.fold_in(_tk, 500 + 29), (12500, 16), jnp.float32)
        tbl_30 = 0.05 * jax.random.normal(jax.random.fold_in(_tk, 500 + 30), (1250, 16), jnp.float32)
        tbl_31 = 0.05 * jax.random.normal(jax.random.fold_in(_tk, 500 + 31), (1250, 16), jnp.float32)
        tbl_32 = 0.05 * jax.random.normal(jax.random.fold_in(_tk, 500 + 32), (125000, 16), jnp.float32)
        tbl_33 = 0.05 * jax.random.normal(jax.random.fold_in(_tk, 500 + 33), (1000, 16), jnp.float32)
        tbl_34 = 0.05 * jax.random.normal(jax.random.fold_in(_tk, 500 + 34), (125000, 16), jnp.float32)
        tbl_35 = 0.05 * jax.random.normal(jax.random.fold_in(_tk, 500 + 35), (1000, 16), jnp.float32)
        tbl_36 = 0.05 * jax.random.normal(jax.random.fold_in(_tk, 500 + 36), (12500, 16), jnp.float32)
        tbl_37 = 0.05 * jax.random.normal(jax.random.fold_in(_tk, 500 + 37), (125000, 16), jnp.float32)
        tbl_38 = 0.05 * jax.random.normal(jax.random.fold_in(_tk, 500 + 38), (1000, 16), jnp.float32)
        _rk = jax.random.fold_in(_tk, 7)
        W_top1 = 0.0693375 * jax.random.normal(jax.random.fold_in(_tk, 801), (208, 512), jnp.float32)
        W_top2 = 0.0441942 * jax.random.normal(jax.random.fold_in(_tk, 802), (512, 256), jnp.float32)
        W_top3 = 0.0625 * jax.random.normal(jax.random.fold_in(_tk, 803), (256, 1), jnp.float32)
        b_top1 = jnp.zeros((512,), jnp.float32)
        b_top2 = jnp.zeros((256,), jnp.float32)
        return (dense_ctx, ids, tbl_0, tbl_1, tbl_2, tbl_3, tbl_4, tbl_5, tbl_6, tbl_7, tbl_8, tbl_9, tbl_10, tbl_11, tbl_12, tbl_13, tbl_14, tbl_15, tbl_16, tbl_17, tbl_18, tbl_19, tbl_20, tbl_21, tbl_22, tbl_23, tbl_24, tbl_25, tbl_26, tbl_27, tbl_28, tbl_29, tbl_30, tbl_31, tbl_32, tbl_33, tbl_34, tbl_35, tbl_36, tbl_37, tbl_38, W_top1, b_top1, W_top2, b_top2, W_top3)
    dense_ctx, ids, tbl_0, tbl_1, tbl_2, tbl_3, tbl_4, tbl_5, tbl_6, tbl_7, tbl_8, tbl_9, tbl_10, tbl_11, tbl_12, tbl_13, tbl_14, tbl_15, tbl_16, tbl_17, tbl_18, tbl_19, tbl_20, tbl_21, tbl_22, tbl_23, tbl_24, tbl_25, tbl_26, tbl_27, tbl_28, tbl_29, tbl_30, tbl_31, tbl_32, tbl_33, tbl_34, tbl_35, tbl_36, tbl_37, tbl_38, W_top1, b_top1, W_top2, b_top2, W_top3 = _rec_inputs()

    def _L0_rec_setup():
        import jax, jax.numpy as jnp
        import numpy as np
        B, F, D = (512, 39, 16)
        L0, L1 = (128, 128)
        H1 = L0 // 2

        def _cin_layer(h, h0, W, b):
            z = jnp.einsum('bhd,bmd->bhmd', h, h0)
            z = z.reshape(z.shape[0], -1, z.shape[-1])
            y = jnp.einsum('oc,bcd->bod', W, z) + b[None, :, None]
            return jax.nn.relu(y)
        key = jax.random.key(seed)
        k0, k1, k2, k3, k4 = jax.random.split(key, 5)
        x = jax.random.normal(k0, (B, F, D), dtype=jnp.float32)
        W0 = jax.random.normal(k1, (L0, F * F), dtype=jnp.float32) * 0.02
        b0 = jnp.zeros((L0,), dtype=jnp.float32)
        W1 = jax.random.normal(k2, (L1, H1 * F), dtype=jnp.float32) * 0.02
        b1 = jnp.zeros((L1,), dtype=jnp.float32)
        return {'x': x, 'W0': W0, 'b0': b0, 'W1': W1, 'b1': b1}
    _L0_rec_all = _L0_rec_setup()
    _L0_rec_in = {k: v for k, v in _L0_rec_all.items() if k in ('W0', 'b0', 'W1', 'b1')}
    del _L0_rec_all
    return {'dense_ctx': dense_ctx, 'ids': ids, 'tbl_0': tbl_0, 'tbl_1': tbl_1, 'tbl_2': tbl_2, 'tbl_3': tbl_3, 'tbl_4': tbl_4, 'tbl_5': tbl_5, 'tbl_6': tbl_6, 'tbl_7': tbl_7, 'tbl_8': tbl_8, 'tbl_9': tbl_9, 'tbl_10': tbl_10, 'tbl_11': tbl_11, 'tbl_12': tbl_12, 'tbl_13': tbl_13, 'tbl_14': tbl_14, 'tbl_15': tbl_15, 'tbl_16': tbl_16, 'tbl_17': tbl_17, 'tbl_18': tbl_18, 'tbl_19': tbl_19, 'tbl_20': tbl_20, 'tbl_21': tbl_21, 'tbl_22': tbl_22, 'tbl_23': tbl_23, 'tbl_24': tbl_24, 'tbl_25': tbl_25, 'tbl_26': tbl_26, 'tbl_27': tbl_27, 'tbl_28': tbl_28, 'tbl_29': tbl_29, 'tbl_30': tbl_30, 'tbl_31': tbl_31, 'tbl_32': tbl_32, 'tbl_33': tbl_33, 'tbl_34': tbl_34, 'tbl_35': tbl_35, 'tbl_36': tbl_36, 'tbl_37': tbl_37, 'tbl_38': tbl_38, 'W_top1': W_top1, 'b_top1': b_top1, 'W_top2': W_top2, 'b_top2': b_top2, 'W_top3': W_top3, 'L0_rec_W0': _L0_rec_in['W0'], 'L0_rec_b0': _L0_rec_in['b0'], 'L0_rec_W1': _L0_rec_in['W1'], 'L0_rec_b1': _L0_rec_in['b1']}

def reference(dense_ctx, ids, tbl_0, tbl_1, tbl_2, tbl_3, tbl_4, tbl_5, tbl_6, tbl_7, tbl_8, tbl_9, tbl_10, tbl_11, tbl_12, tbl_13, tbl_14, tbl_15, tbl_16, tbl_17, tbl_18, tbl_19, tbl_20, tbl_21, tbl_22, tbl_23, tbl_24, tbl_25, tbl_26, tbl_27, tbl_28, tbl_29, tbl_30, tbl_31, tbl_32, tbl_33, tbl_34, tbl_35, tbl_36, tbl_37, tbl_38, W_top1, b_top1, W_top2, b_top2, W_top3, L0_rec_W0, L0_rec_b0, L0_rec_W1, L0_rec_b1):
    import jax
    import jax.numpy as jnp

    def _L0_rec_ref(x, W0, b0, W1, b1):
        import jax, jax.numpy as jnp
        import numpy as np
        B, F, D = (512, 39, 16)
        L0, L1 = (128, 128)
        H1 = L0 // 2

        def _cin_layer(h, h0, W, b):
            z = jnp.einsum('bhd,bmd->bhmd', h, h0)
            z = z.reshape(z.shape[0], -1, z.shape[-1])
            y = jnp.einsum('oc,bcd->bod', W, z) + b[None, :, None]
            return jax.nn.relu(y)
        h0 = x
        y0 = _cin_layer(h0, h0, W0, b0)
        next_hidden, direct0 = (y0[:, :H1, :], y0[:, H1:, :])
        direct1 = _cin_layer(next_hidden, h0, W1, b1)
        result = jnp.sum(jnp.concatenate([direct0, direct1], axis=1), axis=-1)
        return result
    e = jnp.stack([tbl_0[ids[:, 0]], tbl_1[ids[:, 1]], tbl_2[ids[:, 2]], tbl_3[ids[:, 3]], tbl_4[ids[:, 4]], tbl_5[ids[:, 5]], tbl_6[ids[:, 6]], tbl_7[ids[:, 7]], tbl_8[ids[:, 8]], tbl_9[ids[:, 9]], tbl_10[ids[:, 10]], tbl_11[ids[:, 11]], tbl_12[ids[:, 12]], tbl_13[ids[:, 13]], tbl_14[ids[:, 14]], tbl_15[ids[:, 15]], tbl_16[ids[:, 16]], tbl_17[ids[:, 17]], tbl_18[ids[:, 18]], tbl_19[ids[:, 19]], tbl_20[ids[:, 20]], tbl_21[ids[:, 21]], tbl_22[ids[:, 22]], tbl_23[ids[:, 23]], tbl_24[ids[:, 24]], tbl_25[ids[:, 25]], tbl_26[ids[:, 26]], tbl_27[ids[:, 27]], tbl_28[ids[:, 28]], tbl_29[ids[:, 29]], tbl_30[ids[:, 30]], tbl_31[ids[:, 31]], tbl_32[ids[:, 32]], tbl_33[ids[:, 33]], tbl_34[ids[:, 34]], tbl_35[ids[:, 35]], tbl_36[ids[:, 36]], tbl_37[ids[:, 37]], tbl_38[ids[:, 38]]], axis=1)
    z = _L0_rec_ref(e, L0_rec_W0, L0_rec_b0, L0_rec_W1, L0_rec_b1)
    z = z.reshape(z.shape[0], -1)
    h = jnp.concatenate([z, dense_ctx], axis=1)
    h = jnp.maximum(h @ W_top1 + b_top1, 0.0)
    h = jnp.maximum(h @ W_top2 + b_top2, 0.0)
    y = h @ W_top3
    return y

_drawn_inputs = setup_inputs


def setup_inputs(seed=0):
    import zlib

    import numpy as np

    out = dict(_drawn_inputs(seed))
    spreads = {'b_top1': (0.0, 0.8),
     'b_top2': (0.0, 0.343),
     'L0_rec_b0': (0.0, 0.1),
     'L0_rec_b1': (0.0, 0.1)}
    factors = {'tbl_0': 8.0,
     'tbl_1': 8.0,
     'tbl_2': 8.0,
     'tbl_3': 8.0,
     'tbl_4': 8.0,
     'tbl_5': 8.0,
     'tbl_6': 8.0,
     'tbl_7': 8.0,
     'tbl_8': 8.0,
     'tbl_9': 8.0,
     'tbl_10': 8.0,
     'tbl_11': 8.0,
     'tbl_12': 8.0,
     'tbl_13': 8.0,
     'tbl_14': 8.0,
     'tbl_15': 8.0,
     'tbl_16': 8.0,
     'tbl_17': 8.0,
     'tbl_18': 8.0,
     'tbl_19': 8.0,
     'tbl_20': 8.0,
     'tbl_21': 8.0,
     'tbl_22': 8.0,
     'tbl_23': 8.0,
     'tbl_24': 8.0,
     'tbl_25': 8.0,
     'tbl_26': 8.0,
     'tbl_27': 8.0,
     'tbl_28': 8.0,
     'tbl_29': 8.0,
     'tbl_30': 8.0,
     'tbl_31': 8.0,
     'tbl_32': 8.0,
     'tbl_33': 8.0,
     'tbl_34': 8.0,
     'tbl_35': 8.0,
     'tbl_36': 8.0,
     'tbl_37': 8.0,
     'tbl_38': 8.0,
     'L0_rec_W0': 8.0,
     'L0_rec_W1': 3.694}
    for name, (base, spread) in spreads.items():
        noise = np.random.default_rng([zlib.crc32(name.encode()), seed]).standard_normal(out[name].shape)
        drawn = base * np.exp(spread * noise) if base else spread * noise
        out[name] = jnp.asarray(drawn.astype(out[name].dtype))
    for name, factor in factors.items():
        out[name] = (out[name] * factor).astype(out[name].dtype)
    return out
```

```python
import concourse.bass as bass
from concourse import mybir
from contextlib import ExitStack

B, F, D = 2048, 39, 16
H1, L0, L1 = 64, 128, 128
DENSE, N1, N2 = 16, 512, 256
BT = 128
NBT = B // BT
TD = 4
COLS = TD * BT
TPB = D // TD
TILES = NBT * TPB
GROUPS, PER_GROUP, PARTS = 4, 10, 3
EXTRA = 128 - 3 * F
C0 = 6
C1 = 20
STEPS = [(0, i) for i in range(C0 // 2)] + [(1, i) for i in range(C1 // 2)]
LAST_STEPS = STEPS[C0 // 2:]
SPLIT = {(0, 0), (0, 2), (1, 0), (1, 1), (1, 3), (1, 4), (1, 6), (1, 7), (1, 9)}
LAG = 4
SUB_LAG = 2
NZ, NZH, NZP = 4, 6, 4
NLEFT = 2
P_T, P_A = 2, 8
P_E, P_Y1, P_Y0, P_AE = 3, 5, 8, 9
GATHERS = [13, 13, 13, 0]


def layer0_pairs():
    out = {h: [(h + s) % F for s in range(1, (F + 1) // 2)] for h in range(F)}
    chosen = [k * F // EXTRA for k in range(EXTRA)]
    gained = {s: 0 for s in chosen}
    for h in range(F):
        if h not in gained:
            s = min((x for x in out[h] if x in gained), key=lambda x: gained[x])
            out[h].remove(s)
            out[s].append(h)
            gained[s] += 1
    slots = 3 * C0
    chosen.sort(key=lambda s: -len(out[s]))
    left = [p % F for p in range(3 * F)] + chosen
    chunks = []
    for c in range(C0):
        rows = [out[p % F][3 * c + p // F] for p in range(3 * F)]
        rows += [out[s][slots + c] for s in chosen if slots + c < len(out[s])]
        chunks.append(rows)
    assert len({frozenset((left[p], m)) for rows in chunks for p, m in enumerate(rows)}) == F * (F - 1) // 2
    return left, chunks


def schedule():
    steps = [(0, 0, i) for i in range(C0 // 2)]
    for t in range(TILES):
        here = LAST_STEPS if t == TILES - 1 else STEPS
        steps += [(t + 1 - layer, layer, i) for layer, i in here]
    return steps


def layer1_chunks(i):
    g = 2 * (i % 2)
    return [(g, i // 2), (g + 1, i // 2)]


def dlrm_cin_program(nc, dense_t, ids, tables, w0_a, w0_b, b0, w1, b1, wt1, bt1, wt2, bt2, wt3,
                     sel_pairs, sel_left, sel_layer1, identity, out):
    f32, f32r, bf16, i32 = mybir.dt.float32, mybir.dt.float32r, mybir.dt.bfloat16, mybir.dt.int32
    ALU, ACT = mybir.AluOpType, mybir.ActivationFunctionType
    left, chunks0 = layer0_pairs()
    rows0 = [len(rows) for rows in chunks0]
    order = schedule()
    number = {s: n for n, s in enumerate(order)}
    split_steps = [n for n, (_, layer, i) in enumerate(order) if (layer, i) in SPLIT]
    plain_steps = [n for n, (_, layer, i) in enumerate(order) if (layer, i) not in SPLIT]
    split_rank = {n: k for k, n in enumerate(split_steps)}
    plain_rank = {n: k for k, n in enumerate(plain_steps)}
    STEPS_B = TPB * len(STEPS)
    SPLITS_B = TPB * len(SPLIT)
    assert SPLITS_B % NZ == 0 and SPLITS_B % NZH == 0 and (STEPS_B - SPLITS_B) % NZP == 0 and STEPS_B % 2 == 0

    def count(bt, value, per):
        if isinstance(bt, int):
            return value
        assert value > 0
        return bt * per + (value - per)

    def wait(eng, sem, value):
        if not isinstance(value, int) or value > 0:
            eng.wait_ge(sem, value)

    ctx = ExitStack()
    with ctx:
        def sb(name, shape, dt):
            return ctx.enter_context(nc.sbuf_tensor(name, shape, dt))

        def sem(name):
            return ctx.enter_context(nc.semaphore(name))

        ident = sb("ident", [128, 128], bf16)
        sel0 = sb("sel0", [128, C0, 128], bf16)
        sela = sb("sela", [128, 128], bf16)
        sel1 = sb("sel1", [128, C1 // GROUPS, 128], bf16)
        w0s = sb("w0s", [128, C0 + 1, L0], f32)
        w0q = sb("w0q", [128, C0, L0], f32)
        w0h = sb("w0h", [128, C0, L0], f32r)
        w0l = sb("w0l", [128, C0, L0], f32r)
        w1s = sb("w1s", [128, C1, L1], f32)
        w1h = sb("w1h", [128, C1, L1], f32r)
        w1l = sb("w1l", [128, C1, L1], f32r)
        bias0 = sb("bias0", [128, 1], f32)
        bias1 = sb("bias1", [128, 1], f32)
        top1a = sb("top1a", [128, N1], f32)
        top1b = sb("top1b", [128, N1], f32)
        biast1 = sb("biast1", [128, N1 // 128], f32)
        top2 = sb("top2", [128, N1 // 128, N2], f32)
        biast2 = sb("biast2", [128, N2 // 128], f32)
        top3 = sb("top3", [128, N2 // 128], f32)
        idx = [sb(f"idx{k}", [128, F], i32) for k in range(2)]
        rows = [sb(f"rows{k}", [128, GROUPS * PER_GROUP, D], f32) for k in range(2)]
        one = sb("one", [128, 1], f32)
        settled = sb("settled", [1, 1], f32)
        rest1 = sb("rest1", [128, TD, GROUPS, PER_GROUP], f32)
        rest2 = sb("rest2", [128, TD, GROUPS, PER_GROUP], f32)
        parts = sb("parts", [128, TPB, TD, 128], bf16)
        ep = sb("ep", [128, TPB, COLS], bf16)
        left_e = sb("left_e", [128, NLEFT, COLS], f32)
        squares = sb("squares", [F, NLEFT, COLS], f32)
        y2 = sb("y2", [128, TPB, COLS], f32)
        relu0 = sb("relu0", [128, TPB, COLS], f32)
        relu1 = sb("relu1", [128, TPB, COLS], f32)
        z = sb("z", [128, NZ, 2, COLS], f32)
        zh = sb("zh", [128, NZH, 2, COLS], f32r)
        zl = sb("zl", [128, NZH, 2, COLS], f32r)
        zp = sb("zp", [128, NZP, 2, COLS], f32)
        suma = [sb(f"suma{k}", [128, COLS], f32) for k in range(2)]
        sumb = [sb(f"sumb{k}", [128, COLS], f32) for k in range(2)]
        feat_a = sb("feat_a", [128, B], f32)
        feat_b = sb("feat_b", [128, B], f32)
        assert NZ == N1 // 128 and NZP >= 4 and N2 // 128 == 2
        hid1 = z[:, :, :, :].rearrange("p (a b) c n -> p a (b c) n", a=2)
        hid2 = zp[:, 0:2, :, :]
        score = zp[0:1, 2:4, :, :].rearrange("p a b n -> p (a b n)")

        ps = ctx.enter_context(nc.psum_tensor("ps", [128, 8, 512], f32))
        rep = [ps[:, 0:2, :], ps[:, 2:4, :]]
        acc0, acc1, tr, lrep = ps[:, 4, :], ps[:, 5, :], ps[:, 6, :], ps[:, 7, :]

        consts_in = sem("consts_in")
        w_in = sem("w_in")
        mlp_in = sem("mlp_in")
        dense_in = [sem(f"dense_in{k}") for k in range(B // 512)]
        idx_in = [sem(f"idx_in{k}") for k in range(2)]
        gathered = [sem(f"gathered{k}") for k in range(2)]
        zeroed = sem("zeroed")
        folded = sem("folded")
        w_high = sem("w_high")
        w_ready = sem("w_ready")
        pool_did = sem("pool_did")
        parts_made = sem("parts_made")
        tr_done = sem("tr_done")
        ep_made = sem("ep_made")
        lrep_done = sem("lrep_done")
        left_made = sem("left_made")
        rep_done = sem("rep_done")
        z_made = sem("z_made")
        zh_made = sem("zh_made")
        zl_made = sem("zl_made")
        w_done = sem("w_done")
        y2_half = sem("y2_half")
        acc0_read = sem("acc0_read")
        y2_made = sem("y2_made")
        acc1_read = sem("acc1_read")
        relu_read = [sem(f"relu_read{k}") for k in range(2)]
        feat_made = sem("feat_made")
        h1_done = sem("h1_done")
        h1_made = sem("h1_made")
        h2_done = sem("h2_done")
        h2_made = sem("h2_made")
        s_done = sem("s_done")
        s_made = sem("s_made")
        stored = sem("stored")

        block = ctx.enter_context(nc.Block())
        CONSTS, WEIGHTS, MLPS = 6, 3, 7
        NBLK = B // 512

        @block.sync
        def _(sp):
            for k in range(2):
                sp.dma_start(idx[k][:, :], ids[k * BT:(k + 1) * BT, :]).then_inc(idx_in[k], 16)
            for tile, src in ((ident[:, :], identity), (sel0[:, :, :], sel_pairs), (sela[:, :], sel_left),
                              (sel1[:, :, :], sel_layer1), (bias0[:, :], b0), (bias1[:, :], b1)):
                sp.dma_start(tile, src).then_inc(consts_in, 16)
            for tile, src in ((w0s[:, :, :], w0_a), (w0q[:, :, :], w0_b), (w1s[:, :, :], w1)):
                sp.dma_start(tile, src).then_inc(w_in, 16)
            sp.wait_ge(zeroed, 1)
            for tile, src in ((top1a[:, :], wt1[H1:H1 + L1, :]), (top1b[H1:128, :], wt1[0:H1, :]),
                              (top1b[0:DENSE, :], wt1[H1 + L1:, :]), (biast1[:, :], bt1), (top2[:, :, :], wt2.rearrange("(k p) n -> p k n", p=128)),
                              (biast2[:, :], bt2), (top3[:, :], wt3)):
                sp.dma_start(tile, src).then_inc(mlp_in, 16)
            with sp.Fori(1, NBT // 2) as pair:
                for k in range(2):
                    sp.wait_ge(gathered[k], pair * (16 * F))
                    sp.dma_start(idx[k][:, :], ids[bass.ds((pair * 2 + k) * BT, BT), :]).then_inc(idx_in[k], 16)
            for blk in range(NBLK):
                cols = slice(blk * 512, (blk + 1) * 512)
                sp.wait_ge(feat_made, 2 * (blk + 1) * (512 // BT))
                sp.dma_start(feat_b[0:DENSE, cols], dense_t[:, cols]).then_inc(dense_in[blk], 16)
            for blk in range(NBLK):
                sp.wait_ge(s_made, blk + 1)
                sp.dma_start(out[blk * 512:(blk + 1) * 512, :].rearrange("n o -> o n"),
                             score[0:1, blk * 512:(blk + 1) * 512]).then_inc(stored, 16)
            sp.wait_ge(stored, 16 * NBLK)

        @block.gpsimd
        def _(pool):
            links = [0]
            per_pair = [0]

            def link(ins):
                links[0] += 1
                ins.then_inc(pool_did, 1)

            def linked(pair):
                if isinstance(pair, int):
                    wait(pool, pool_did, links[0])
                else:
                    pool.wait_ge(pool_did, pair * per_pair[0] + (links[0] - per_pair[0]))

            def settle(pair):
                linked(pair)
                link(nc.gpsimd.tensor_tensor(settled[:, :], one[0:1, :], one[0:1, :], ALU.add))

            def rounded(to, of):
                return nc.gpsimd.tensor_tensor(to, of, one[:, :].unsqueeze(2).unsqueeze(3).to_broadcast(
                    [128, TD, GROUPS, PER_GROUP]), ALU.mult)

            def lookup(pair, k, first, n):
                settle(pair)
                for f in range(first, first + n):
                    pool.indirect_dma_start(rows[k][:, f, :], None, tables[f],
                                            bass.IndirectOffsetOnAxis(ap=idx[k][:, f:f + 1], axis=0))\
                        .then_inc(gathered[k], 16)

            def split(pair, k, q):
                src = rows[k][:, :, q * TD:(q + 1) * TD].rearrange("p (g j) d -> p d g j", g=GROUPS)
                to = [parts[:, q, :, :].rearrange("p d (g r) -> p d g r", g=GROUPS)
                      [:, :, :, n * PER_GROUP:(n + 1) * PER_GROUP] for n in range(PARTS)]
                link(rounded(to[0], src))
                linked(pair)
                link(nc.gpsimd.tensor_tensor(rest1[:, :, :, :], src, to[0], ALU.subtract))
                linked(pair)
                link(rounded(to[1], rest1[:, :, :, :]))
                linked(pair)
                link(nc.gpsimd.tensor_tensor(rest2[:, :, :, :], rest1[:, :, :, :], to[1], ALU.subtract))
                linked(pair)
                rounded(to[2], rest2[:, :, :, :]).then_inc(parts_made, 1)

            relus = [relu0, relu1]
            feats = [feat_b, feat_a]

            def sum_first():
                for l in range(2):
                    nc.gpsimd.tensor_tensor(suma[l][:, :], relus[l][:, 0, :], relus[l][:, 1, :], ALU.add)\
                        .then_inc(relu_read[l], 1)

            def sum_rest(pair, bt):
                wait(pool, feat_made, bt * 2)
                for l in range(2):
                    nc.gpsimd.tensor_tensor(sumb[l][:, :], relus[l][:, 2, :], relus[l][:, 3, :], ALU.add)\
                        .then_inc(relu_read[l], 1)
                for l in range(2):
                    pool.wait_ge(relu_read[l], bt * 2 + 2)
                    link(nc.gpsimd.tensor_tensor(suma[l][:, :], suma[l][:, :], sumb[l][:, :], ALU.add))
                linked(pair)
                for l in range(2):
                    link(nc.gpsimd.tensor_tensor(sumb[l][:, 0:2 * BT], suma[l][:, 0:2 * BT],
                                                 suma[l][:, 2 * BT:4 * BT], ALU.add))
                linked(pair)
                for l in range(2):
                    nc.gpsimd.tensor_tensor(feats[l][:, bass.ds(bt * BT, BT)], sumb[l][:, 0:BT],
                                            sumb[l][:, BT:2 * BT], ALU.add).then_inc(feat_made, 1)

            def iteration(pair, k, q):
                whole = isinstance(pair, int)
                bt = pair * 2 + k
                bt0 = bt if whole else 2 + k
                t0 = TPB * bt0 + q

                def c(value, per_btile):
                    return value if whole else pair * (2 * per_btile) + (value - 2 * per_btile)
                if not whole or bt + 2 < NBT:
                    if q == 0:
                        pool.wait_ge(idx_in[k], c(16 * (bt0 // 2 + 2), 8))
                        pool.wait_ge(parts_made, c(TPB * (bt0 + 1), TPB))
                    if GATHERS[q]:
                        lookup(pair, k, sum(GATHERS[:q]), GATHERS[q])
                if not whole or t0 + TPB < TILES:
                    o = 1 - k
                    if q == 0:
                        pool.wait_ge(gathered[o], c(16 * F * ((bt0 + 1) // 2 + 1), 8 * F))
                    pool.wait_ge(tr_done, c(t0 + 1, TPB))
                    split(pair, o, q)
                if q == 0 and bt0 > 0:
                    pool.wait_ge(acc1_read, c(t0, TPB))
                    pool.wait_ge(acc0_read, c(t0, TPB))
                    sum_rest(pair, bt - 1)
                if q == 2:
                    pool.wait_ge(acc1_read, c(t0, TPB))
                    pool.wait_ge(acc0_read, c(t0, TPB))
                    if bt0 > 0:
                        linked(pair)
                    sum_first()

            def both(pair):
                for k in range(2):
                    for q in range(TPB):
                        iteration(pair, k, q)

            nc.gpsimd.memset(one[:, :], 1.0)
            nc.gpsimd.memset(parts[:, :, :, :], 0.0)
            for k in range(2):
                nc.gpsimd.memset(rows[k][:, F:, :], 0.0)
            nc.gpsimd.memset(top1b[:, :], 0.0)
            nc.gpsimd.memset(relu0[:, :, :], 0.0).then_inc(zeroed, 1)
            pool.wait_ge(zeroed, 1)
            pool.wait_ge(idx_in[0], 16)
            lookup(0, 0, 0, F)
            pool.wait_ge(gathered[0], 16 * F)
            for q in range(TPB):
                split(0, 0, q)
            pool.wait_ge(idx_in[1], 16)
            lookup(0, 1, 0, F)
            both(0)
            per_pair[0] = 2 * (TPB * 4 + 4 + sum(n > 0 for n in GATHERS))
            with pool.Fori(1, NBT // 2 - 1) as pair:
                both(pair)
            links[0] += per_pair[0] * (NBT // 2 - 3)
            both(NBT // 2 - 1)
            pool.wait_ge(acc1_read, TILES)
            pool.wait_ge(acc0_read, TILES)
            sum_rest(NBT // 2 - 1, NBT - 1)

        def iterations(eng, body):
            for q in range(TPB):
                body(0, q)
            with eng.Fori(1, NBT - 1) as bt:
                for q in range(TPB):
                    body(bt, q)
            for q in range(TPB):
                body(NBT - 1, q)

        @block.tensor
        def _(pe):
            def transpose_parts(bt, t):
                pe.wait_ge(parts_made, count(bt, t + 1, TPB))
                wait(pe, ep_made, count(bt, t, TPB) if t else 0)
                for d in range(TD):
                    last = nc.tensor.matmul(tr[:, d * BT:(d + 1) * BT], parts[:, t % TPB, d, :], ident[:, :],
                                            start=True, stop=True)
                last.then_inc(tr_done, 1)

            def replicate_left(bt, t):
                pe.wait_ge(ep_made, count(bt, t + 1, TPB))
                wait(pe, left_made, count(bt, t, TPB) if t else 0)
                nc.tensor.matmul(lrep, sela[:, :], ep[:, t % TPB, :], start=True, stop=True)\
                    .then_inc(lrep_done, 1)

            def replicate(bt, n):
                t, layer, i = order[n]
                wait(pe, z_made, count(bt, n - 1, STEPS_B) if n >= 2 else 0)
                if layer == 0:
                    for c in range(2):
                        last = nc.tensor.matmul(rep[n % 2][:, c, :], sel0[:, 2 * i + c, :], ep[:, t % TPB, :],
                                                start=True, stop=True)
                else:
                    for c, (g, r) in enumerate(layer1_chunks(i)):
                        at = slice(32 * g, 32 * g + PARTS * PER_GROUP)
                        last = nc.tensor.matmul(rep[n % 2][:, c, :], sel1[at, r, :], ep[at, t % TPB, :],
                                                start=True, stop=True)
                last.then_inc(rep_done, 1)

            def products(bt, n):
                t, layer, i = order[n]
                acc = acc1 if layer else acc0
                first, final = i == 0, i == (C1 if layer else C0) // 2 - 1
                if first:
                    wait(pe, acc1_read if layer else acc0_read, count(bt, t, TPB) if t else 0)
                if first and not layer:
                    pe.wait_ge(left_made, count(bt, t + 1, TPB))
                    nc.tensor.matmul(acc, w0s[0:F, C0, :], squares[:, t % NLEFT, :], start=True, stop=False)
                if n in split_rank:
                    pe.wait_ge(zl_made, count(bt, split_rank[n] + 1, SPLITS_B))
                else:
                    pe.wait_ge(z_made, count(bt, n + 1, STEPS_B))
                for c in range(2):
                    if layer:
                        g, r = layer1_chunks(i)[c]
                        chunk = C1 // GROUPS * g + r
                        k = H1 if chunk == C1 - 1 else 128
                        whole, high, low = w1s, w1h, w1l
                    else:
                        chunk, k = 2 * i + c, rows0[2 * i + c]
                        whole, high, low = w0s, w0h, w0l
                    start, stop = first and layer == 1 and c == 0, final and c == 1
                    if n in split_rank:
                        s = split_rank[n] % NZH
                        nc.tensor.matmul(acc, low[0:k, chunk, :], zh[0:k, s, c, :], start=start, stop=False)
                        nc.tensor.matmul(acc, high[0:k, chunk, :], zl[0:k, s, c, :], start=False, stop=False)
                        last = nc.tensor.matmul(acc, high[0:k, chunk, :], zh[0:k, s, c, :],
                                                start=False, stop=stop)
                    else:
                        last = nc.tensor.matmul(acc, whole[0:k, chunk, :],
                                                zp[0:k, plain_rank[n] % NZP, c, :], start=start, stop=stop)
                last.then_inc(w_done, 1)

            def iteration(bt, q):
                t = TPB * (bt if isinstance(bt, int) else 1) + q
                here = LAST_STEPS if t == TILES - 1 else STEPS
                n0 = number[(t + 1 - here[0][0], *here[0])]
                for p in range(len(here)):
                    replicate(bt, n0 + p)
                    if n0 + p >= LAG:
                        products(bt, n0 + p - LAG)
                    if p == P_T and t + 2 < TILES:
                        transpose_parts(bt, t + 2)
                    if p == P_A and t + 2 < TILES:
                        replicate_left(bt, t + 2)

            pe.wait_ge(consts_in, 16 * CONSTS)
            for t in range(2):
                transpose_parts(0, t)
                replicate_left(0, t)
            pe.wait_ge(w_ready, 1)
            for n in range(C0 // 2):
                replicate(0, n)
            iterations(pe, iteration)
            for n in range(len(order) - LAG, len(order)):
                products(0, n)

            pe.wait_ge(mlp_in, 16 * MLPS)

            def mlp1(blk):
                cols = slice(blk * 512, (blk + 1) * 512)
                pe.wait_ge(feat_made, 2 * (blk + 1) * (512 // BT))
                pe.wait_ge(dense_in[blk], 16)
                for m in range(N1 // 128):
                    wait(pe, h1_made, (blk - 1) * (N1 // 128) + m + 1)
                    ms = slice(m * 128, (m + 1) * 128)
                    nc.tensor.matmul(ps[:, m, :], top1a[:, ms], feat_a[:, cols], start=True, stop=False)
                    nc.tensor.matmul(ps[:, m, :], top1b[:, ms], feat_b[:, cols], start=False, stop=True)\
                        .then_inc(h1_done, 1)

            def mlp2(blk):
                pe.wait_ge(h1_made, (blk + 1) * (N1 // 128))
                for m in range(N2 // 128):
                    wait(pe, h2_made, (blk - 1) * (N2 // 128) + m + 1)
                    for k in range(N1 // 128):
                        last = nc.tensor.matmul(ps[:, 4 + m, :], top2[:, k, m * 128:(m + 1) * 128],
                                                hid1[:, blk % 2, k, :], start=k == 0, stop=k == N1 // 128 - 1)
                    last.then_inc(h2_done, 1)

            def mlp3(blk):
                pe.wait_ge(h2_made, (blk + 1) * (N2 // 128))
                wait(pe, s_made, blk)
                for k in range(N2 // 128):
                    last = nc.tensor.matmul(ps[0:1, 6, :], top3[:, k:k + 1], hid2[:, blk % 2, k, :],
                                            start=k == 0, stop=k == N2 // 128 - 1)
                last.then_inc(s_done, 1)

            pe.wait_ge(acc1_read, TILES)
            mlp1(0)
            for blk in range(NBLK):
                if blk + 1 < NBLK:
                    mlp1(blk + 1)
                mlp2(blk)
                mlp3(blk)

        @block.scalar
        def _(act):
            def high_part(bt, n):
                k = split_rank[n]
                act.wait_ge(z_made, count(bt, n + 1, STEPS_B))
                if k >= NZH:
                    act.wait_ge(w_done, count(bt, split_steps[k - NZH] + 1, STEPS_B))
                nc.scalar.activation(zh[:, k % NZH, :, :], z[:, k % NZ, :, :], ACT.Copy).then_inc(zh_made, 1)

            def parts_out(bt, t):
                act.wait_ge(tr_done, count(bt, t + 1, TPB))
                if t >= TPB:
                    act.wait_ge(rep_done, count(bt, number[(t - TPB, 1, C1 // 2 - 1)] + 1, STEPS_B))
                nc.scalar.activation(ep[:, t % TPB, :], tr, ACT.Copy).then_inc(ep_made, 1)

            def left_out(bt, t):
                act.wait_ge(lrep_done, count(bt, t + 1, TPB))
                if t >= NLEFT:
                    act.wait_ge(w_done, count(bt, number[(t - NLEFT, 0, C0 // 2 - 1)] + 1, STEPS_B))
                nc.scalar.activation(left_e[:, t % NLEFT, :], lrep, ACT.Copy)
                nc.scalar.activation(squares[:, t % NLEFT, :], lrep[0:F, :], ACT.Square).then_inc(left_made, 1)

            def layer0_out(bt, t):
                act.wait_ge(w_done, count(bt, number[(t, 0, C0 // 2 - 1)] + 1, STEPS_B))
                if t >= TPB:
                    act.wait_ge(z_made, count(bt, number[(t - TPB, 1, C1 // 2 - 1)] + 1, STEPS_B))
                    act.wait_ge(relu_read[0], count(bt, (t - TPB) // 2 + 1, 2))
                s = t % TPB
                nc.scalar.activation(y2[0:H1, s, :], acc0[0:H1, :], ACT.Relu, bias=bias0[0:H1, :])\
                    .then_inc(y2_half, 1)
                nc.scalar.activation(relu0[H1:128, s, :], acc0[H1:128, :], ACT.Relu, bias=bias0[H1:128, :])\
                    .then_inc(acc0_read, 1)
                act.wait_ge(y2_half, count(bt, t + 1, TPB))
                nc.scalar.activation(y2[H1:128, s, :], y2[0:H1, s, :], ACT.Copy).then_inc(y2_made, 1)

            def layer1_out(bt, t):
                act.wait_ge(w_done, count(bt, number[(t, 1, C1 // 2 - 1)] + 1, STEPS_B))
                if t >= TPB:
                    act.wait_ge(relu_read[1], count(bt, (t - TPB) // 2 + 1, 2))
                nc.scalar.activation(relu1[:, t % TPB, :], acc1, ACT.Relu, bias=bias1[:, :])\
                    .then_inc(acc1_read, 1)

            def iteration(bt, q):
                t = TPB * (bt if isinstance(bt, int) else 1) + q
                here = LAST_STEPS if t == TILES - 1 else STEPS
                n0 = number[(t + 1 - here[0][0], *here[0])]
                for p, step in enumerate(here):
                    if t == 0 and step == (1, 0):
                        layer0_out(0, 0)
                    if step in SPLIT:
                        high_part(bt, n0 + p)
                    if p == P_E and t + 2 < TILES:
                        parts_out(bt, t + 2)
                    if p == P_Y1 and t > 0:
                        layer1_out(bt, t - 1)
                    if p == P_Y0 and t + 1 < TILES:
                        layer0_out(bt, t + 1)
                    if p == P_AE and t + 2 < TILES:
                        left_out(bt, t + 2)

            act.wait_ge(folded, 1)
            nc.scalar.activation(w0h[:, :, :], w0s[:, 0:C0, :], ACT.Copy)
            nc.scalar.activation(w1h[:, :, :], w1s[:, :, :], ACT.Copy).then_inc(w_high, 1)
            act.wait_ge(consts_in, 16 * CONSTS)
            for t in range(2):
                parts_out(0, t)
                left_out(0, t)
            for n in range(C0 // 2):
                if n in split_rank:
                    high_part(0, n)
            iterations(act, iteration)
            layer1_out(NBT - 1, TILES - 1)

            act.wait_ge(mlp_in, 16 * MLPS)
            for blk in range(NBLK):
                for m in range(N1 // 128):
                    act.wait_ge(h1_done, blk * (N1 // 128) + m + 1)
                    if blk >= 2:
                        act.wait_ge(h2_done, (blk - 1) * (N2 // 128))
                    nc.scalar.activation(hid1[:, blk % 2, m, :], ps[:, m, :], ACT.Relu,
                                         bias=biast1[:, m:m + 1]).then_inc(h1_made, 1)

        @block.vector
        def _(dve):
            def pair_products(bt, n):
                t, layer, i = order[n]
                dve.wait_ge(rep_done, count(bt, n + 1, STEPS_B))
                if i == 0:
                    dve.wait_ge(y2_made if layer else left_made, count(bt, t + 1, TPB))
                if n in split_rank:
                    k = split_rank[n]
                    if k >= NZ:
                        dve.wait_ge(zl_made, count(bt, k - NZ + 1, SPLITS_B))
                    to = z[:, k % NZ, :, :]
                else:
                    k = plain_rank[n]
                    if k >= NZP:
                        dve.wait_ge(w_done, count(bt, plain_steps[k - NZP] + 1, STEPS_B))
                    to = zp[:, k % NZP, :, :]
                factor = (y2[:, t % TPB, :] if layer else left_e[:, t % NLEFT, :]).unsqueeze(1).to_broadcast([128, 2, COLS])
                nc.vector.tensor_tensor(to, rep[n % 2], factor, ALU.mult).then_inc(z_made, 1)

            def low_part(bt, n):
                k = split_rank[n]
                dve.wait_ge(zh_made, count(bt, k + 1, SPLITS_B))
                if k >= NZH:
                    dve.wait_ge(w_done, count(bt, split_steps[k - NZH] + 1, STEPS_B))
                nc.vector.tensor_tensor(zl[:, k % NZH, :, :], z[:, k % NZ, :, :],
                                        zh[:, k % NZH, :, :].bitcast(f32), ALU.subtract).then_inc(zl_made, 1)

            def iteration(bt, q):
                t = TPB * (bt if isinstance(bt, int) else 1) + q
                here = LAST_STEPS if t == TILES - 1 else STEPS
                n0 = number[(t + 1 - here[0][0], *here[0])]
                for n in range(n0, n0 + len(here)):
                    pair_products(bt, n)
                    if n - SUB_LAG in split_rank:
                        low_part(bt, n - SUB_LAG)

            dve.wait_ge(w_in, 16 * WEIGHTS)
            nc.vector.tensor_tensor(w0s[:, 0:C0, :], w0s[:, 0:C0, :], w0q[:, :, :], ALU.add).then_inc(folded, 1)
            dve.wait_ge(w_high, 1)
            nc.vector.tensor_tensor(w0l[:, :, :], w0s[:, 0:C0, :], w0h[:, :, :].bitcast(f32), ALU.subtract)
            nc.vector.tensor_tensor(w1l[:, :, :], w1s[:, :, :], w1h[:, :, :].bitcast(f32), ALU.subtract)\
                .then_inc(w_ready, 1)
            for n in range(C0 // 2):
                pair_products(0, n)
                if n - SUB_LAG in split_rank:
                    low_part(0, n - SUB_LAG)
            iterations(dve, iteration)
            for n in range(len(order) - SUB_LAG, len(order)):
                if n in split_rank:
                    low_part(NBT - 1, n)

            dve.wait_ge(mlp_in, 16 * MLPS)
            for blk in range(NBLK):
                for m in range(N2 // 128):
                    dve.wait_ge(h2_done, blk * (N2 // 128) + m + 1)
                    if blk >= 2:
                        dve.wait_ge(s_done, blk - 1)
                    nc.vector.tensor_scalar(hid2[:, blk % 2, m, :], ps[:, 4 + m, :], biast2[:, m:m + 1], 0.0,
                                            ALU.add, ALU.max).then_inc(h2_made, 1)
                dve.wait_ge(s_done, blk + 1)
                nc.vector.tensor_copy(score[0:1, blk * 512:(blk + 1) * 512], ps[0:1, 6, :]).then_inc(s_made, 1)


def kernel(**inputs):
    import numpy as np
    import concourse.bacc as bacc
    from concourse.bass_utils import run_bass_kernel_spmd

    bf16 = np.dtype("bfloat16")
    left, chunks0 = layer0_pairs()
    def part_row(f, n):
        return 32 * (f // PER_GROUP) + n * PER_GROUP + f % PER_GROUP

    sel_pairs = np.zeros((128, C0, 128), bf16)
    sel_left = np.zeros((128, 128), bf16)
    sel_layer1 = np.zeros((128, C1 // GROUPS, 128), bf16)
    for n in range(PARTS):
        for c, rows in enumerate(chunks0):
            for p, m in enumerate(rows):
                sel_pairs[part_row(m, n), c, p] = 1
        for p, h in enumerate(left):
            sel_left[part_row(h, n), p] = 1
        for m in range(F):
            j = m % PER_GROUP
            sel_layer1[part_row(m, n), j // 2, (j % 2) * H1:(j % 2 + 1) * H1] = 1

    w0 = np.asarray(inputs["L0_rec_W0"])
    w0_a = np.zeros((128, C0 + 1, L0), w0.dtype)
    w0_b = np.zeros((128, C0, L0), w0.dtype)
    for c, rows in enumerate(chunks0):
        for p, m in enumerate(rows):
            w0_a[p, c, :] = w0[:, left[p] * F + m]
            w0_b[p, c, :] = w0[:, m * F + left[p]]
    for m in range(F):
        w0_a[m, C0, :] = w0[:, m * F + m]
    w1 = np.asarray(inputs["L0_rec_W1"])
    rows1 = w1.reshape(L1, H1, F).transpose(2, 1, 0)
    w1_c = np.zeros((C1, 2, H1, L1), w1.dtype)
    w1_c.reshape(2 * C1, H1, L1)[0:F] = rows1
    w1_c = w1_c.reshape(C1, 128, L1).transpose(1, 0, 2)

    arrays = {
        "dense_t": np.asarray(inputs["dense_ctx"]).T,
        "ids": np.asarray(inputs["ids"]),
        **{f"tbl_{f}": np.asarray(inputs[f"tbl_{f}"]) for f in range(F)},
        "w0_a": w0_a, "w0_b": w0_b, "b0": np.asarray(inputs["L0_rec_b0"]).reshape(L0, 1),
        "w1": w1_c, "b1": np.asarray(inputs["L0_rec_b1"]).reshape(L1, 1),
        "wt1": np.asarray(inputs["W_top1"]), "bt1": np.asarray(inputs["b_top1"]).reshape(N1 // 128, 128).T,
        "wt2": np.asarray(inputs["W_top2"]), "bt2": np.asarray(inputs["b_top2"]).reshape(N2 // 128, 128).T,
        "wt3": np.asarray(inputs["W_top3"]).reshape(N2 // 128, 128).T,
        "sel_pairs": sel_pairs, "sel_left": sel_left, "sel_layer1": sel_layer1,
        "identity": np.eye(128, dtype=np.float32).astype(bf16),
    }
    arrays = {n: np.ascontiguousarray(a) for n, a in arrays.items()}

    nc = bacc.Bacc("TRN2", target_bir_lowering=False, num_devices=1)
    ap = {n: nc.dram_tensor(n, a.shape, mybir.dt.from_np(a.dtype), kind="ExternalInput").ap()
          for n, a in arrays.items()}
    out = nc.dram_tensor("scores", (B, 1), mybir.dt.float32, kind="ExternalOutput").ap()
    dlrm_cin_program(nc, ap["dense_t"], ap["ids"], [ap[f"tbl_{f}"] for f in range(F)], ap["w0_a"], ap["w0_b"],
                     ap["b0"], ap["w1"], ap["b1"], ap["wt1"], ap["bt1"], ap["wt2"], ap["bt2"], ap["wt3"],
                     ap["sel_pairs"], ap["sel_left"], ap["sel_layer1"], ap["identity"], out)
    r = run_bass_kernel_spmd(nc, [arrays], core_ids=[0])
    return r.results[0]["scores"]
```

```python
import concourse.bass as bass
from concourse import mybir
from contextlib import ExitStack

B, F, D = 2048, 39, 16
H1, L0, L1 = 64, 128, 128
DENSE, N1, N2 = 16, 512, 256
BT = 128
NBT = B // BT
TD = 4
COLS = TD * BT
TPB = D // TD
TILES = NBT * TPB
GROUPS, PER_GROUP, PARTS = 4, 10, 3
EXTRA = 128 - 3 * F
C0 = 6
C1 = (F + 1) // 2
STEPS = [(0, 0), (0, 1), (1, 0), (1, 1), (0, 2)] + [(1, i) for i in range(2, C1 // 2)]
PLAIN = {(0, 0), (0, 1)}
SPLIT = set(STEPS) - PLAIN
LAST_STEPS = [step for step in STEPS if step[0] == 1]
POOLED = {(1, 2), (1, 5), (1, 8)}
LAG = 6
SUB_LAG = 2
NREP = 3
NZ, NZH, NZP = 4, 8, 4
NLEFT = 2
P_T, P_A = 6, 8
P_E, P_Y1, P_Y0, P_AE, P_SE = P_T - 1, LAG - 1, LAG + 5, P_A - 1, 7
MLP_AT = [(2, 1), (2, 8), (3, 4)]
MLP_OUT_AT = [(q, p - 1) for q, p in MLP_AT]
SUM_FIRST_AT = [(2, 7), (2, 8)]
SUM_REST_AT = [(0, 7), (0, 8), (0, 10), (0, 11), (1, 0), (1, 1), (1, 2), (1, 3)]
LOOKUP_AT = [1, 2, 3, 4, 6, 7, 8, 9, 10, 11]
SPLIT_AT = [0, 1, 4]
ROUND_AT = [2, 6]
P_SQ = 11


def layer0_pairs():
    out = {h: [(h + s) % F for s in range(1, (F + 1) // 2)] for h in range(F)}
    chosen = [k * F // EXTRA for k in range(EXTRA)]
    gained = {s: 0 for s in chosen}
    for h in range(F):
        if h not in gained:
            s = min((x for x in out[h] if x in gained), key=lambda x: gained[x])
            out[h].remove(s)
            out[s].append(h)
            gained[s] += 1
    slots = 3 * C0
    chosen.sort(key=lambda s: -len(out[s]))
    left = [p % F for p in range(3 * F)] + chosen
    chunks = []
    for c in range(C0):
        rows = [out[p % F][3 * c + p // F] for p in range(3 * F)]
        rows += [out[s][slots + c] for s in chosen if slots + c < len(out[s])]
        chunks.append(rows)
    assert len({frozenset((left[p], m)) for rows in chunks for p, m in enumerate(rows)}) == F * (F - 1) // 2
    return left, chunks


def schedule():
    steps = [(0, 0, i) for i in range(C0 // 2)]
    for t in range(TILES):
        here = LAST_STEPS if t == TILES - 1 else STEPS
        steps += [(t + 1 - layer, layer, i) for layer, i in here]
    return steps


def splits_at(t):
    late = {0: [], 1: [(4, 6)], 2: [(5, 0), (6, 6)], 3: [(7, 0)]}
    return late[t] if t < TPB else [(t + TPB, 0)] if t + TPB < TILES else []


def lookups_at(t, p):
    at = [(q, x) for q in range(TPB) for x in LOOKUP_AT] if t >= TPB else \
         [(1, x) for x in range(7, len(STEPS))] + [(q, x) for q in (2, 3) for x in range(len(STEPS))]
    if (t % TPB, p) not in at or t >= TILES - 2 * TPB:
        return []
    j, n = at.index((t % TPB, p)), min(len(at), F)
    return range(j * F // n, min((j + 1) * F // n, F))


def banks():
    users = [("parts", 0), ("left", 0)] + [("step", n) for n in range(C0 // 2)] + [("parts", 1), ("left", 1)]
    n = C0 // 2
    for t in range(TILES):
        for p in range(len(LAST_STEPS if t == TILES - 1 else STEPS)):
            users.append(("step", n))
            n += 1
            if t + 2 < TILES and p == P_T:
                users.append(("parts", t + 2))
            if t + 2 < TILES and p == P_A:
                users.append(("left", t + 2))
            if t >= TPB and (t % TPB, p) in MLP_AT:
                users.append((f"mlp {MLP_AT.index((t % TPB, p))}", t // TPB - 1))
    return users + [(f"mlp {k}", NBT - 1) for k in range(3)]


def dlrm_cin_program(nc, dense_t, ids, tables, w0_a, w0_b, b0, w1, b1, wt1, bt1, wt2, bt2, wt3,
                     sel_pairs, sel_left, sel_layer1, row_mask, identity, out):
    f32, f32r, bf16, i32 = mybir.dt.float32, mybir.dt.float32r, mybir.dt.bfloat16, mybir.dt.int32
    ALU, ACT = mybir.AluOpType, mybir.ActivationFunctionType
    left, chunks0 = layer0_pairs()
    rows0 = [len(rows) for rows in chunks0]
    order = schedule()
    number = {s: n for n, s in enumerate(order)}
    split_steps = [n for n, (_, layer, i) in enumerate(order) if (layer, i) in SPLIT]
    plain_steps = [n for n, (_, layer, i) in enumerate(order) if (layer, i) not in SPLIT]
    split0 = [2 * i + c for layer, i in sorted(SPLIT) if layer == 0 for c in range(2)] + [C0]
    split_rank = {n: k for k, n in enumerate(split_steps)}
    plain_rank = {n: k for k, n in enumerate(plain_steps)}
    STEPS_B = TPB * len(STEPS)
    SPLITS_B = TPB * len(SPLIT)
    users = banks()
    turn = {user: k for k, user in enumerate(users)}
    POOLED_B = TPB * len(POOLED)

    def pooled(n):
        return order[n][1:] in POOLED and order[n][0] >= TPB - 1

    low_rank = {n: sum(pooled(m) == pooled(n) for m in split_steps[:k])
                for k, n in enumerate(split_steps)}
    for per, ring in ((SPLITS_B, NZ), (SPLITS_B, NZH), (STEPS_B - SPLITS_B, NZP), (STEPS_B + 2 * TPB + 3, NREP)):
        assert 2 * per % ring == 0

    def count(bt, value, per):
        if isinstance(bt, int):
            return value
        assert value > 0
        return bt * (2 * per) + value

    def wait(eng, sem, value):
        if not isinstance(value, int) or value > 0:
            eng.wait_ge(sem, value)

    ctx = ExitStack()
    with ctx:
        def sb(name, shape, dt):
            return ctx.enter_context(nc.sbuf_tensor(name, shape, dt))

        def sem(name):
            return ctx.enter_context(nc.semaphore(name))

        ident = sb("ident", [128, 128], bf16)
        sel0 = sb("sel0", [128, C0, 128], bf16)
        sela = sb("sela", [128, 128], bf16)
        sel1 = sb("sel1", [128, C1, 128], bf16)
        w0s = sb("w0s", [128, C0 + 1, L0], f32)
        w0h = sb("w0h", [128, len(split0), L0], f32r)
        w0l = sb("w0l", [128, len(split0), L0], f32r)
        w1h = sb("w1h", [128, C1, L1], f32r)
        w1l = sb("w1l", [128, C1, L1], f32r)
        wsq_both = sb("wsq_both", [128, L0], f32r)
        wsq_high = sb("wsq_high", [128, L0], f32r)
        wlast_both = sb("wlast_both", [128, L1], f32r)
        wlast_high = sb("wlast_high", [128, L1], f32r)
        wtmp = sb("wtmp", [128, 2, 128], f32)
        rowmask = sb("rowmask", [128, 4], f32)
        bias0 = sb("bias0", [128, 1], f32)
        bias1 = sb("bias1", [128, 1], f32)
        top1a = sb("top1a", [128, N1], f32)
        top1b = sb("top1b", [128, N1], f32)
        biast1 = sb("biast1", [128, N1 // 128], f32)
        top2 = sb("top2", [128, N1 // 128, N2], f32)
        biast2 = sb("biast2", [128, N2 // 128], f32)
        top3 = sb("top3", [128, N2 // 128], f32)
        idx = [sb(f"idx{k}", [128, F], i32) for k in range(2)]
        rows = [sb(f"rows{k}", [128, GROUPS * PER_GROUP, D], f32) for k in range(2)]
        one = sb("one", [128, 1], f32)
        settled = sb("settled", [1, 1], f32)
        rest1 = sb("rest1", [128, TD, GROUPS, PER_GROUP], f32)
        rest2 = sb("rest2", [128, TD, GROUPS, PER_GROUP], f32)
        parts = sb("parts", [128, TPB, TD, 128], bf16)
        ep = sb("ep", [128, TPB, COLS], bf16)
        left_e = sb("left_e", [128, NLEFT, COLS], f32)
        sq = sb("sq", [128, NLEFT, COLS], f32)
        sqh = sb("sqh", [128, NLEFT, COLS], f32r)
        sql = sb("sql", [128, NLEFT, COLS], f32r)
        y2 = sb("y2", [128, TPB, COLS], f32)
        relu0 = sb("relu0", [128, TPB, COLS], f32)
        relu1 = sb("relu1", [128, TPB, COLS], f32)
        z = sb("z", [128, NZ, 2, COLS], f32)
        zh = sb("zh", [128, NZH, 2, COLS], f32r)
        zl = sb("zl", [128, NZH, 2, COLS], f32r)
        zp = sb("zp", [128, NZP, 2, COLS], f32)
        stage = z[:, :, :, :].rearrange("p s c n -> p (s c n)")
        w1s = stage[:, 0:C1 * L1].rearrange("p (c o) -> p c o", o=L1)
        w0q = stage[:, C1 * L1:(C1 + C0) * L1].rearrange("p (c o) -> p c o", o=L0)
        suma = [sb(f"suma{k}", [128, COLS], f32) for k in range(2)]
        sumb = [sb(f"sumb{k}", [128, COLS], f32) for k in range(2)]
        feat_a = sb("feat_a", [128, BT], f32)
        feat_b = sb("feat_b", [128, BT], f32)
        hid1 = sb("hid1", [128, N1 // 128, BT], f32)
        hid2 = sb("hid2", [128, N2 // 128, BT], f32)
        score = sb("score", [1, BT], f32)

        ps = ctx.enter_context(nc.psum_tensor("ps", [128, 8, 512], f32))
        acc0, acc1 = ps[:, 2 * NREP, :], ps[:, 2 * NREP + 1, :]

        def slot(user):
            k = turn[user] % NREP
            return ps[:, 2 * k:2 * k + 2, :]

        consts_in = sem("consts_in")
        w_in = sem("w_in")
        mlp_in = sem("mlp_in")
        dense_in = sem("dense_in")
        idx_in = [sem(f"idx_in{k}") for k in range(2)]
        gathered = [sem(f"gathered{k}") for k in range(2)]
        zeroed = sem("zeroed")
        folded = sem("folded")
        w_high = sem("w_high")
        w_low = sem("w_low")
        w_ready = sem("w_ready")
        pool_did = sem("pool_did")
        rest_made = sem("rest_made")
        part2_made = sem("part2_made")
        parts_made = sem("parts_made")
        tr_done = sem("tr_done")
        ep_made = sem("ep_made")
        lrep_done = sem("lrep_done")
        left_made = sem("left_made")
        sq_made = sem("sq_made")
        sql_made = sem("sql_made")
        rep_done = sem("rep_done")
        z_made = sem("z_made")
        zh_made = sem("zh_made")
        zl_made = sem("zl_made")
        zl_pool = sem("zl_pool")
        w_done = sem("w_done")
        y2_half = sem("y2_half")
        acc0_read = sem("acc0_read")
        y2_made = sem("y2_made")
        acc1_read = sem("acc1_read")
        relu_read = [sem(f"relu_read{k}") for k in range(2)]
        feat_made = sem("feat_made")
        h1_done = sem("h1_done")
        h1_made = sem("h1_made")
        h2_done = sem("h2_done")
        h2_made = sem("h2_made")
        s_done = sem("s_done")
        s_made = sem("s_made")
        stored = sem("stored")

        out_row = out.rearrange("n o -> o n")
        block = ctx.enter_context(nc.Block())
        CONSTS, WEIGHTS, MLPS = 7, 3, 7

        def read_of(bt, user):
            what, n = user
            made, per = {"step": (z_made, STEPS_B), "parts": (ep_made, TPB), "left": (left_made, TPB),
                         "mlp 0": (h1_made, 1), "mlp 1": (h2_made, 1), "mlp 2": (s_made, 1)}[what]
            return made, count(bt, n + 1, per)

        def low_done(n):
            return (zl_pool, POOLED_B) if pooled(n) else (zl_made, SPLITS_B - POOLED_B)

        @block.sync
        def _(sp):
            for k in range(2):
                sp.dma_start(idx[k][:, :], ids[k * BT:(k + 1) * BT, :]).then_inc(idx_in[k], 16)
            for tile, src in ((ident[:, :], identity), (sel0[:, :, :], sel_pairs), (sela[:, :], sel_left),
                              (sel1[:, :, :], sel_layer1), (rowmask[:, :], row_mask), (bias0[:, :], b0),
                              (bias1[:, :], b1)):
                sp.dma_start(tile, src).then_inc(consts_in, 16)
            for tile, src in ((w0s[:, :, :], w0_a), (w0q[:, :, :], w0_b), (w1s[:, :, :], w1)):
                sp.dma_start(tile, src).then_inc(w_in, 16)
            sp.wait_ge(zeroed, 1)
            sp.dma_start(relu0[0:DENSE, 0, 0:BT], dense_t[:, 0:BT]).then_inc(dense_in, 16)
            for tile, src in ((top1a[:, :], wt1[H1:H1 + L1, :]), (top1b[H1:128, :], wt1[0:H1, :]),
                              (top1b[0:DENSE, :], wt1[H1 + L1:, :]), (biast1[:, :], bt1),
                              (top2[:, :, :], wt2.rearrange("(k p) n -> p k n", p=128)),
                              (biast2[:, :], bt2), (top3[:, :], wt3)):
                sp.dma_start(tile, src).then_inc(mlp_in, 16)
            with sp.Fori(1, NBT // 2) as pair:
                for k in range(2):
                    sp.wait_ge(gathered[k], pair * (16 * F))
                    sp.dma_start(idx[k][:, :], ids[bass.ds((pair * 2 + k) * BT, BT), :]).then_inc(idx_in[k], 16)
            sp.wait_ge(stored, 16 * NBT)

        @block.gpsimd
        def _(pool):
            links = [0]
            per_pair = [0]

            def link(ins):
                links[0] += 1
                ins.then_inc(pool_did, 1)

            def linked(pair):
                if isinstance(pair, int):
                    wait(pool, pool_did, links[0])
                else:
                    pool.wait_ge(pool_did, pair * per_pair[0] + (links[0] - per_pair[0]))

            def settle(pair):
                linked(pair)
                link(nc.gpsimd.tensor_tensor(settled[:, :], one[0:1, :], one[0:1, :], ALU.add))

            def rounded(to, of):
                return nc.gpsimd.tensor_tensor(to, of, one[:, :].unsqueeze(2).unsqueeze(3).to_broadcast(
                    [128, TD, GROUPS, PER_GROUP]), ALU.mult)

            def lookup(k, f):
                pool.indirect_dma_start(rows[k][:, f, :], None, tables[f],
                                        bass.IndirectOffsetOnAxis(ap=idx[k][:, f:f + 1], axis=0))\
                    .then_inc(gathered[k], 16)

            def split(pair, k, q, part, tiles):
                src = rows[k][:, :, q * TD:(q + 1) * TD].rearrange("p (g j) d -> p d g j", g=GROUPS)
                to = [parts[:, q, :, :].rearrange("p d (g r) -> p d g r", g=GROUPS)
                      [:, :, :, n * PER_GROUP:(n + 1) * PER_GROUP] for n in range(PARTS)]
                if part == 0:
                    link(rounded(to[0], src))
                if part == 1:
                    linked(pair)
                    nc.gpsimd.tensor_tensor(rest1[:, :, :, :], src, to[0], ALU.subtract).then_inc(rest_made, 1)
                if part == 2:
                    pool.wait_ge(part2_made, tiles)
                    nc.gpsimd.tensor_tensor(rest2[:, :, :, :], rest1[:, :, :, :], to[1], ALU.subtract)\
                        .then_inc(rest_made, 1)

            relus = [relu0, relu1]
            feats = [feat_b, feat_a]

            def sum_first(l):
                nc.gpsimd.tensor_tensor(suma[l][:, :], relus[l][:, 0, :], relus[l][:, 1, :], ALU.add)\
                    .then_inc(relu_read[l], 1)

            def sum_rest(pair, bt, part):
                l = part % 2
                if part == 0:
                    wait(pool, feat_made, bt * 2)
                if part < 2:
                    nc.gpsimd.tensor_tensor(sumb[l][:, :], relus[l][:, 2, :], relus[l][:, 3, :], ALU.add)\
                        .then_inc(relu_read[l], 1)
                elif part < 4:
                    pool.wait_ge(relu_read[l], bt * 2 + 2)
                    link(nc.gpsimd.tensor_tensor(suma[l][:, :], suma[l][:, :], sumb[l][:, :], ALU.add))
                elif part < 6:
                    linked(pair)
                    link(nc.gpsimd.tensor_tensor(sumb[l][:, 0:2 * BT], suma[l][:, 0:2 * BT],
                                                 suma[l][:, 2 * BT:4 * BT], ALU.add))
                else:
                    linked(pair)
                    nc.gpsimd.tensor_tensor(feats[l][:, :], sumb[l][:, 0:BT], sumb[l][:, BT:2 * BT],
                                            ALU.add).then_inc(feat_made, 1)

            def low_part(n, c):
                if pooled(n):
                    r = split_rank[n]
                    pool.wait_ge(zh_made, c(r + 1, SPLITS_B))
                    if r >= NZH:
                        pool.wait_ge(w_done, c(split_steps[r - NZH] + 1, STEPS_B))
                    nc.gpsimd.tensor_tensor(zl[:, r % NZH, :, :], z[:, r % NZ, :, :],
                                            zh[:, r % NZH, :, :].bitcast(f32), ALU.subtract)\
                        .then_inc(zl_pool, 1)

            def iteration(pair, k, q):
                whole = isinstance(pair, int)
                bt = pair * 2 + k
                bt0 = bt if whole else 2 + k
                t0 = TPB * bt0 + q

                def c(value, per_btile):
                    assert whole or value > 0
                    return value if whole else pair * (2 * per_btile) + (value - 2 * per_btile)

                here = LAST_STEPS if t0 == TILES - 1 else STEPS
                n0 = number[(t0 + 1 - here[0][0], *here[0])]
                for p in range(len(here)):
                    low_part(n0 + p - SUB_LAG, c)
                    for f in lookups_at(t0, p):
                        if f == 0:
                            pool.wait_ge(idx_in[k], c(16 * (bt0 // 2 + 2), 8))
                            pool.wait_ge(parts_made, c(TPB * (bt0 + 1), TPB))
                            settle(pair)
                        lookup(k, f)
                    for t, later in splits_at(t0):
                        if p - later not in SPLIT_AT:
                            continue
                        if p - later == SPLIT_AT[0]:
                            if t % TPB == 0:
                                pool.wait_ge(gathered[1 - k], c(16 * F * ((bt0 + 1) // 2 + 1), 8 * F))
                            pool.wait_ge(tr_done, c(t + 1 - TPB, TPB))
                            pool.wait_ge(parts_made, c(t, TPB))
                        split(pair, 1 - k, t % TPB, SPLIT_AT.index(p - later), c(t + 1, TPB))
                    if (q, p) in SUM_REST_AT and bt0 > 0:
                        part = SUM_REST_AT.index((q, p))
                        if part == 0:
                            pool.wait_ge(acc1_read, c(t0, TPB))
                            pool.wait_ge(acc0_read, c(t0, TPB))
                        sum_rest(pair, bt - 1, part)
                    if (q, p) in SUM_FIRST_AT:
                        l = SUM_FIRST_AT.index((q, p))
                        if l == 0:
                            pool.wait_ge(acc1_read, c(t0, TPB))
                            pool.wait_ge(acc0_read, c(t0, TPB))
                            pool.wait_ge(dense_in, c(16 * (bt0 + 1), 16))
                            if bt0 > 0:
                                linked(pair)
                        sum_first(l)

            def both(pair):
                for k in range(2):
                    for q in range(TPB):
                        iteration(pair, k, q)

            nc.gpsimd.memset(one[:, :], 1.0)
            nc.gpsimd.memset(parts[:, :, :, :], 0.0)
            for k in range(2):
                nc.gpsimd.memset(rows[k][:, F:, :], 0.0)
            nc.gpsimd.memset(top1b[:, :], 0.0)
            nc.gpsimd.memset(relu0[:, :, :], 0.0).then_inc(zeroed, 1)
            pool.wait_ge(zeroed, 1)
            pool.wait_ge(idx_in[0], 16)
            for f in range(F):
                lookup(0, f)
            pool.wait_ge(gathered[0], 16 * F)
            for q in range(TPB):
                for part in range(3):
                    if part == 0 and q:
                        pool.wait_ge(parts_made, q)
                    split(0, 0, q, part, q + 1)
            pool.wait_ge(idx_in[1], 16)
            for f in range(F):
                lookup(1, f)
            both(0)
            per_pair[0] = 2 * (TPB + 4 + 1)
            with pool.Fori(1, NBT // 2 - 1) as pair:
                both(pair)
            links[0] += per_pair[0] * (NBT // 2 - 3)
            both(NBT // 2 - 1)
            for n in range(len(order) - SUB_LAG, len(order)):
                low_part(n, lambda value, per_btile: value)
            pool.wait_ge(acc0_read, TILES)
            for part in (0, 2, 4, 6):
                sum_rest(NBT // 2 - 1, NBT - 1, part)
            for tile in (TILES - 2, TILES - 1):
                pool.wait_ge(acc1_read, tile + 1)
                pool.wait_ge(relu_read[1], 2 * NBT - 1)
                linked(NBT // 2 - 1)
                link(nc.gpsimd.tensor_tensor(suma[1][:, :], suma[1][:, :], relu1[:, tile % TPB, :], ALU.add))
            for part in (5, 7):
                sum_rest(NBT // 2 - 1, NBT - 1, part)

        assert NBT % 2 == 0

        def iterations(eng, body):
            for q in range(TPB):
                body(0, q)
            with eng.Fori(0, NBT // 2 - 1) as pair:
                for q in range(2 * TPB):
                    body(pair, q)
            for q in range(TPB):
                body(NBT - 1, q)

        @block.tensor
        def _(pe):
            def take_slot(bt, user):
                if turn[user] >= NREP:
                    made, value = read_of(bt, users[turn[user] - NREP])
                    pe.wait_ge(made, value)
                return slot(user)

            def transpose_parts(bt, t):
                tr = take_slot(bt, ("parts", t))
                pe.wait_ge(parts_made, count(bt, t + 1, TPB))
                for d in range(TD):
                    last = nc.tensor.matmul(tr[:, 0, d * BT:(d + 1) * BT], parts[:, t % TPB, d, :], ident[:, :],
                                            start=True, stop=True)
                last.then_inc(tr_done, 1)

            def replicate_left(bt, t):
                lrep = take_slot(bt, ("left", t))
                pe.wait_ge(ep_made, count(bt, t + 1, TPB))
                nc.tensor.matmul(lrep[:, 0, :], sela[:, :], ep[:, t % TPB, :], start=True, stop=True)\
                    .then_inc(lrep_done, 1)

            def replicate(bt, n):
                t, layer, i = order[n]
                rep = take_slot(bt, ("step", n))
                for c in range(2):
                    last = nc.tensor.matmul(rep[:, c, :], (sel1 if layer else sel0)[:, 2 * i + c, :],
                                            ep[:, t % TPB, :], start=True, stop=True)
                last.then_inc(rep_done, 1)

            def products(bt, n):
                t, layer, i = order[n]
                acc = acc1 if layer else acc0
                first, final = i == 0, i == (C1 if layer else C0) // 2 - 1
                if first:
                    wait(pe, acc1_read if layer else acc0_read, count(bt, t, TPB) if t else 0)
                if first and not layer:
                    pe.wait_ge(sql_made, count(bt, t + 1, TPB))
                    nc.tensor.matmul(acc, wsq_both[:, :], sqh[:, t % NLEFT, :], start=True, stop=False)
                    nc.tensor.matmul(acc, wsq_high[:, :], sql[:, t % NLEFT, :], start=False, stop=False)
                if n in split_rank:
                    made, per = low_done(n)
                    pe.wait_ge(made, count(bt, low_rank[n] + 1, per))
                else:
                    pe.wait_ge(z_made, count(bt, n + 1, STEPS_B))
                for c in range(2):
                    chunk = 2 * i + c
                    k = 128 if layer else rows0[chunk]
                    start, stop = first and layer == 1 and c == 0, final and c == 1
                    if n not in split_rank:
                        last = nc.tensor.matmul(acc, w0s[0:k, chunk, :], zp[0:k, plain_rank[n] % NZP, c, :],
                                                start=start, stop=stop)
                        continue
                    s = split_rank[n] % NZH
                    high, low = (w1h[:, chunk, :], w1l[:, chunk, :]) if layer else \
                        (w0h[0:k, split0.index(chunk), :], w0l[0:k, split0.index(chunk), :])
                    if layer and chunk == C1 - 1:
                        nc.tensor.matmul(acc, wlast_high[:, :], zl[:, s, c, :], start=False, stop=False)
                        last = nc.tensor.matmul(acc, wlast_both[:, :], zh[:, s, c, :], start=False, stop=stop)
                        continue
                    nc.tensor.matmul(acc, low, zh[0:k, s, c, :], start=start, stop=False)
                    nc.tensor.matmul(acc, high, zl[0:k, s, c, :], start=False, stop=False)
                    last = nc.tensor.matmul(acc, high, zh[0:k, s, c, :], start=False, stop=stop)
                last.then_inc(w_done, 1)

            def iteration(bt, q):
                t = TPB * (bt if isinstance(bt, int) else 1) + q
                here = LAST_STEPS if t == TILES - 1 else STEPS
                n0 = number[(t + 1 - here[0][0], *here[0])]
                for p in range(len(here)):
                    replicate(bt, n0 + p)
                    if n0 + p >= LAG + C0 // 2:
                        products(bt, n0 + p - LAG)
                    if p == P_T and t + 2 < TILES:
                        transpose_parts(bt, t + 2)
                    if p == P_A and t + 2 < TILES:
                        replicate_left(bt, t + 2)
                    if (t % TPB, p) in MLP_AT and t >= TPB:
                        mlp_layer(bt, t // TPB, MLP_AT.index((t % TPB, p)))

            def mlp_layer(bt, b, layer):
                mlp = take_slot(bt, (f"mlp {layer}", b - 1))[:, 0, :]
                if layer == 0:
                    pe.wait_ge(mlp_in, 16 * MLPS)
                    pe.wait_ge(feat_made, count(bt, 2 * b, 2))
                    for m in range(N1 // 128):
                        ms = slice(m * 128, (m + 1) * 128)
                        nc.tensor.matmul(mlp[:, ms], top1b[:, ms], feat_b[:, :], start=True, stop=False)
                        last = nc.tensor.matmul(mlp[:, ms], top1a[:, ms], feat_a[:, :], start=False, stop=True)
                    last.then_inc(h1_done, 1)
                if layer == 1:
                    pe.wait_ge(h1_made, count(bt, b, 1))
                    for m in range(N2 // 128):
                        ms = slice(m * 128, (m + 1) * 128)
                        for k in range(N1 // 128):
                            last = nc.tensor.matmul(mlp[:, ms], top2[:, k, ms], hid1[:, k, :],
                                                    start=k == 0, stop=k == N1 // 128 - 1)
                    last.then_inc(h2_done, 1)
                if layer == 2:
                    pe.wait_ge(h2_made, count(bt, b, 1))
                    for k in range(N2 // 128):
                        last = nc.tensor.matmul(mlp[0:1, 0:BT], top3[:, k:k + 1], hid2[:, k, :],
                                                start=k == 0, stop=k == N2 // 128 - 1)
                    last.then_inc(s_done, 1)

            pe.wait_ge(consts_in, 16 * CONSTS)
            transpose_parts(0, 0)
            replicate_left(0, 0)
            for n in range(C0 // 2):
                replicate(0, n)
            transpose_parts(0, 1)
            replicate_left(0, 1)
            pe.wait_ge(w_ready, 1)
            for n in range(C0 // 2):
                products(0, n)
            iterations(pe, iteration)
            for n in range(len(order) - LAG, len(order)):
                products(0, n)

            for layer in range(3):
                mlp_layer(NBT, NBT, layer)

        @block.scalar
        def _(act):
            def high_part(bt, n):
                k = split_rank[n]
                act.wait_ge(z_made, count(bt, n + 1, STEPS_B))
                if k >= NZH:
                    act.wait_ge(w_done, count(bt, split_steps[k - NZH] + 1, STEPS_B))
                nc.scalar.activation(zh[:, k % NZH, :, :], z[:, k % NZ, :, :], ACT.Copy).then_inc(zh_made, 1)

            def parts_out(bt, t):
                act.wait_ge(tr_done, count(bt, t + 1, TPB))
                if t >= TPB:
                    act.wait_ge(rep_done, count(bt, number[(t - TPB, 1, C1 // 2 - 1)] + 1, STEPS_B))
                nc.scalar.activation(ep[:, t % TPB, :], slot(("parts", t))[:, 0, :], ACT.Copy)\
                    .then_inc(ep_made, 1)

            def left_out(bt, t):
                act.wait_ge(lrep_done, count(bt, t + 1, TPB))
                if t >= NLEFT:
                    act.wait_ge(w_done, count(bt, number[(t - NLEFT, 0, C0 // 2 - 1)] + 1, STEPS_B))
                nc.scalar.activation(left_e[:, t % NLEFT, :], slot(("left", t))[:, 0, :], ACT.Copy)\
                    .then_inc(left_made, 1)

            def squares_out(bt, t):
                act.wait_ge(left_made, count(bt, t + 1, TPB))
                if t >= NLEFT:
                    act.wait_ge(sql_made, count(bt, t - NLEFT + 1, TPB))
                nc.scalar.activation(sq[:, t % NLEFT, :], left_e[:, t % NLEFT, :], ACT.Square)
                nc.scalar.activation(sqh[:, t % NLEFT, :], left_e[:, t % NLEFT, :], ACT.Square)\
                    .then_inc(sq_made, 1)

            def round_rest(bt, t, part):
                act.wait_ge(rest_made, count(bt, 2 * t + part, 2 * TPB))
                to = parts[:, t % TPB, :, :].rearrange("p d (g r) -> p d g r", g=GROUPS)
                nc.scalar.activation(to[:, :, :, part * PER_GROUP:(part + 1) * PER_GROUP],
                                     (rest1 if part == 1 else rest2)[:, :, :, :], ACT.Copy)\
                    .then_inc(part2_made if part == 1 else parts_made, 1)

            def layer0_out(bt, t):
                act.wait_ge(w_done, count(bt, number[(t, 0, C0 // 2 - 1)] + 1, STEPS_B))
                if t >= TPB:
                    act.wait_ge(z_made, count(bt, number[(t - TPB, 1, C1 // 2 - 1)] + 1, STEPS_B))
                    act.wait_ge(relu_read[0], count(bt, (t - TPB) // 2 + 1, 2))
                s = t % TPB
                if s == 0 and t:
                    cols = bass.ds(count(bt, t // TPB, 1) * BT, BT)
                    act.dma_start(relu0[0:DENSE, 0, 0:BT], dense_t[:, cols]).then_inc(dense_in, 16)
                nc.scalar.activation(y2[0:H1, s, :], acc0[0:H1, :], ACT.Relu, bias=bias0[0:H1, :])\
                    .then_inc(y2_half, 1)
                nc.scalar.activation(relu0[H1:128, s, :], acc0[H1:128, :], ACT.Relu, bias=bias0[H1:128, :])\
                    .then_inc(acc0_read, 1)
                act.wait_ge(y2_half, count(bt, t + 1, TPB))
                nc.scalar.activation(y2[H1:128, s, :], y2[0:H1, s, :], ACT.Copy).then_inc(y2_made, 1)

            def layer1_out(bt, t):
                act.wait_ge(w_done, count(bt, number[(t, 1, C1 // 2 - 1)] + 1, STEPS_B))
                if t >= TPB:
                    act.wait_ge(relu_read[1], count(bt, (t - TPB) // 2 + 1, 2))
                nc.scalar.activation(relu1[:, t % TPB, :], acc1, ACT.Relu, bias=bias1[:, :])\
                    .then_inc(acc1_read, 1)

            def iteration(bt, q):
                t = TPB * (bt if isinstance(bt, int) else 1) + q
                here = LAST_STEPS if t == TILES - 1 else STEPS
                n0 = number[(t + 1 - here[0][0], *here[0])]
                for p, step in enumerate(here):
                    if step in SPLIT:
                        high_part(bt, n0 + p)
                    if p == P_E and t + 2 < TILES:
                        parts_out(bt, t + 2)
                    if p == P_Y1 and t > 0:
                        layer1_out(bt, t - 1)
                    if p == P_Y0 and t + 1 < TILES:
                        layer0_out(bt, t + 1)
                    if p == P_AE and t + 2 < TILES:
                        left_out(bt, t + 2)
                    if p == P_SE and t + 2 < TILES:
                        squares_out(bt, t + 2)
                    for ahead, later in splits_at(t):
                        if p - later in ROUND_AT:
                            round_rest(bt, ahead, 1 + ROUND_AT.index(p - later))
                    if (t % TPB, p) == (TPB - 1, len(LAST_STEPS) - 1) and t >= TPB:
                        act.wait_ge(stored, count(bt, 16 * (t // TPB), 16))
                    if (t % TPB, p) in MLP_OUT_AT and t >= TPB:
                        mlp_out(bt, t // TPB, MLP_OUT_AT.index((t % TPB, p)))

            def mlp_out(bt, b, layer):
                mlp = slot((f"mlp {layer}", b - 1))[:, 0, :]
                done, made, hid, bias, n = [(h1_done, h1_made, hid1, biast1, N1 // 128),
                                            (h2_done, h2_made, hid2, biast2, N2 // 128),
                                            (s_done, s_made, None, None, 0)][layer]
                act.wait_ge(done, count(bt, b, 1))
                for m in range(n):
                    last = nc.scalar.activation(hid[:, m, :], mlp[:, m * 128:(m + 1) * 128], ACT.Relu,
                                                bias=bias[:, m:m + 1])
                if layer == 2:
                    last = nc.scalar.activation(score[:, :], mlp[0:1, 0:BT], ACT.Copy)
                last.then_inc(made, 1)
                if layer == 2:
                    act.wait_ge(s_made, count(bt, b, 1))
                    act.dma_start(out_row[:, bass.ds(count(bt, b, 1) * BT - BT, BT)], score[:, :])\
                        .then_inc(stored, 16)

            act.wait_ge(mlp_in, 16 * MLPS)
            act.wait_ge(folded, 1)
            for k, chunk in enumerate(split0):
                nc.scalar.activation(w0h[:, k, :], w0s[:, chunk, :], ACT.Copy)
            nc.scalar.activation(w1h[:, :, :], w1s[:, :, :], ACT.Copy).then_inc(w_high, 1)
            act.wait_ge(consts_in, 16 * CONSTS)
            for t in range(TPB):
                round_rest(0, t, 1)
                if 0 < t <= 2:
                    left_out(0, t - 1)
                round_rest(0, t, 2)
                if 0 < t <= 2:
                    squares_out(0, t - 1)
                if t < 2:
                    parts_out(0, t)
            for n in range(C0 // 2):
                if n in split_rank:
                    high_part(0, n)
            layer0_out(0, 0)
            iterations(act, iteration)
            layer1_out(NBT - 1, TILES - 1)

            for layer in range(3):
                mlp_out(NBT, NBT, layer)

        @block.vector
        def _(dve):
            def pair_products(bt, n):
                t, layer, i = order[n]
                dve.wait_ge(rep_done, count(bt, n + 1, STEPS_B))
                if i == 0:
                    dve.wait_ge(y2_made if layer else left_made, count(bt, t + 1, TPB))
                if n in split_rank:
                    k = split_rank[n]
                    if k >= NZ:
                        low, per = low_done(split_steps[k - NZ])
                        dve.wait_ge(low, count(bt, low_rank[split_steps[k - NZ]] + 1, per))
                    to = z[:, k % NZ, :, :]
                else:
                    k = plain_rank[n]
                    if k >= NZP:
                        dve.wait_ge(w_done, count(bt, plain_steps[k - NZP] + 1, STEPS_B))
                    to = zp[:, k % NZP, :, :]
                factor = y2[:, t % TPB, :] if layer else left_e[:, t % NLEFT, :]
                nc.vector.tensor_tensor(to, slot(("step", n)), factor.unsqueeze(1).to_broadcast([128, 2, COLS]),
                                        ALU.mult).then_inc(z_made, 1)

            def square_low_part(bt, t):
                dve.wait_ge(sq_made, count(bt, t + 1, TPB))
                if t >= NLEFT:
                    dve.wait_ge(w_done, count(bt, number[(t - NLEFT, 0, C0 // 2 - 1)] + 1, STEPS_B))
                s = t % NLEFT
                nc.vector.tensor_tensor(sql[:, s, :], sq[:, s, :], sqh[:, s, :].bitcast(f32), ALU.subtract)\
                    .then_inc(sql_made, 1)

            def low_part(bt, n):
                if n not in split_rank or pooled(n):
                    return
                k = split_rank[n]
                dve.wait_ge(zh_made, count(bt, k + 1, SPLITS_B))
                if k >= NZH:
                    dve.wait_ge(w_done, count(bt, split_steps[k - NZH] + 1, STEPS_B))
                nc.vector.tensor_tensor(zl[:, k % NZH, :, :], z[:, k % NZ, :, :],
                                        zh[:, k % NZH, :, :].bitcast(f32), ALU.subtract).then_inc(zl_made, 1)

            def iteration(bt, q):
                t = TPB * (bt if isinstance(bt, int) else 1) + q
                here = LAST_STEPS if t == TILES - 1 else STEPS
                n0 = number[(t + 1 - here[0][0], *here[0])]
                for n in range(n0, n0 + len(here)):
                    pair_products(bt, n)
                    if n - n0 == P_SQ and t + 2 < TILES:
                        square_low_part(bt, t + 2)
                    if n - SUB_LAG >= C0 // 2:
                        low_part(bt, n - SUB_LAG)

            dve.wait_ge(w_in, 16 * WEIGHTS)
            nc.vector.tensor_tensor(w0s[:, 0:C0, :], w0s[:, 0:C0, :], w0q[:, :, :], ALU.add).then_inc(folded, 1)
            dve.wait_ge(w_high, 1)
            for k, chunk in enumerate(split0):
                nc.vector.tensor_tensor(w0l[:, k, :], w0s[:, chunk, :], w0h[:, k, :].bitcast(f32), ALU.subtract)
            nc.vector.tensor_tensor(w1l[:, :, :], w1s[:, :, :], w1h[:, :, :].bitcast(f32), ALU.subtract)\
                .then_inc(w_low, 1)
            dve.wait_ge(consts_in, 16 * CONSTS)
            dve.wait_ge(w_low, 1)
            for k, (high, low, to_both, to_high) in enumerate((
                    (w0h[:, len(split0) - 1, :], w0l[:, len(split0) - 1, :], wsq_both, wsq_high),
                    (w1h[:, C1 - 1, :], w1l[:, C1 - 1, :], wlast_both, wlast_high))):
                in_high, in_low = rowmask[:, 2 * k:2 * k + 1], rowmask[:, 2 * k + 1:2 * k + 2]
                nc.vector.tensor_scalar(to_high[:, :], high.bitcast(f32), in_high, None, ALU.mult)
                nc.vector.tensor_scalar(wtmp[:, k, :], high.bitcast(f32), in_high, None, ALU.mult)\
                    .then_inc(w_low, 1)
                dve.wait_ge(w_low, 2 + k)
                last = nc.vector.scalar_tensor_tensor(to_both[:, :], low.bitcast(f32), in_low, wtmp[:, k, :],
                                                      ALU.mult, ALU.add)
            last.then_inc(w_ready, 1)
            square_low_part(0, 0)
            for n in range(C0 // 2):
                pair_products(0, n)
            square_low_part(0, 1)
            for n in range(C0 // 2):
                low_part(0, n)
            iterations(dve, iteration)
            for n in range(len(order) - SUB_LAG, len(order)):
                low_part(NBT - 1, n)


def kernel(**inputs):
    import numpy as np
    import concourse.bacc as bacc
    from concourse.bass_utils import run_bass_kernel_spmd

    bf16 = np.dtype("bfloat16")
    left, chunks0 = layer0_pairs()
    def part_row(f, n):
        return 32 * (f // PER_GROUP) + n * PER_GROUP + f % PER_GROUP

    sel_pairs = np.zeros((128, C0, 128), bf16)
    sel_left = np.zeros((128, 128), bf16)
    sel_layer1 = np.zeros((128, C1, 128), bf16)
    for n in range(PARTS):
        for c, rows in enumerate(chunks0):
            for p, m in enumerate(rows):
                sel_pairs[part_row(m, n), c, p] = 1
        for p, h in enumerate(left):
            sel_left[part_row(h, n), p] = 1
        for m in range(F):
            sel_layer1[part_row(m, n), m // 2, (m % 2) * H1:(m % 2 + 1) * H1] = 1
        sel_layer1[part_row(F - 1, n), C1 - 1, :] = 1
    row_mask = np.zeros((128, 4), np.float32)
    for k, rows in enumerate((F, H1)):
        row_mask[0:rows, 2 * k] = 1
        row_mask[rows:2 * rows, 2 * k + 1] = 1

    w0 = np.asarray(inputs["L0_rec_W0"])
    w0_a = np.zeros((128, C0 + 1, L0), w0.dtype)
    w0_b = np.zeros((128, C0, L0), w0.dtype)
    for c, rows in enumerate(chunks0):
        for p, m in enumerate(rows):
            w0_a[p, c, :] = w0[:, left[p] * F + m]
            w0_b[p, c, :] = w0[:, m * F + left[p]]
    for m in range(F):
        w0_a[m, C0, :] = w0_a[F + m, C0, :] = w0[:, m * F + m]
    w1 = np.asarray(inputs["L0_rec_W1"])
    rows1 = w1.reshape(L1, H1, F).transpose(2, 1, 0)
    w1_c = np.zeros((C1, 2, H1, L1), w1.dtype)
    w1_c.reshape(2 * C1, H1, L1)[0:F] = rows1
    w1_c[C1 - 1, 1] = rows1[F - 1]
    w1_c = w1_c.reshape(C1, 128, L1).transpose(1, 0, 2)

    arrays = {
        "dense_t": np.asarray(inputs["dense_ctx"]).T,
        "ids": np.asarray(inputs["ids"]),
        **{f"tbl_{f}": np.asarray(inputs[f"tbl_{f}"]) for f in range(F)},
        "w0_a": w0_a, "w0_b": w0_b, "b0": np.asarray(inputs["L0_rec_b0"]).reshape(L0, 1),
        "w1": w1_c, "b1": np.asarray(inputs["L0_rec_b1"]).reshape(L1, 1),
        "wt1": np.asarray(inputs["W_top1"]), "bt1": np.asarray(inputs["b_top1"]).reshape(N1 // 128, 128).T,
        "wt2": np.asarray(inputs["W_top2"]), "bt2": np.asarray(inputs["b_top2"]).reshape(N2 // 128, 128).T,
        "wt3": np.asarray(inputs["W_top3"]).reshape(N2 // 128, 128).T,
        "sel_pairs": sel_pairs, "sel_left": sel_left, "sel_layer1": sel_layer1, "row_mask": row_mask,
        "identity": np.eye(128, dtype=np.float32).astype(bf16),
    }
    arrays = {n: np.ascontiguousarray(a) for n, a in arrays.items()}

    nc = bacc.Bacc("TRN2", target_bir_lowering=False, num_devices=1)
    ap = {n: nc.dram_tensor(n, a.shape, mybir.dt.from_np(a.dtype), kind="ExternalInput").ap()
          for n, a in arrays.items()}
    out = nc.dram_tensor("scores", (B, 1), mybir.dt.float32, kind="ExternalOutput").ap()
    dlrm_cin_program(nc, ap["dense_t"], ap["ids"], [ap[f"tbl_{f}"] for f in range(F)], ap["w0_a"], ap["w0_b"],
                     ap["b0"], ap["w1"], ap["b1"], ap["wt1"], ap["bt1"], ap["wt2"], ap["bt2"], ap["wt3"],
                     ap["sel_pairs"], ap["sel_left"], ap["sel_layer1"], ap["row_mask"], ap["identity"], out)
    r = run_bass_kernel_spmd(nc, [arrays], core_ids=[0])
    return r.results[0]["scores"]
```
